# Optimizing a Trainium2 kernel written in Bass

```python
import numpy as np
import jax
import jax.numpy as jnp

def _softmax(x, axis=-1):
    return jax.nn.softmax(x, axis=axis)

def _gelu(x):
    return jax.nn.gelu(x, approximate=True)

def _silu(x):
    return jax.nn.silu(x)

def _sigmoid(x):
    return jax.nn.sigmoid(x)

def _layernorm(x, axis=-1, eps=1e-05):
    m = jnp.mean(x, axis=axis, keepdims=True)
    v = jnp.var(x, axis=axis, keepdims=True)
    return (x - m) / jnp.sqrt(v + eps)

def _scatter_add(tgt, idx, src, axis=0):
    return tgt.at[idx].add(src)

def _segment_sum(src, seg, n):
    return jax.ops.segment_sum(src, seg, n)
kernel_name = 'mk_gnn_resnorm_d2_gnn_r8_2656a6'

def setup_inputs(seed: int=0):
    np.random.seed(seed)
    _w = jnp.asarray

    def _rec_inputs():
        import jax
        import jax.numpy as jnp
        _gk = jax.random.key(seed)
        x = -0.0005121 + 1.001 * jax.random.normal(jax.random.fold_in(_gk, 1), (12500, 32), jnp.float32)
        src = jax.random.randint(jax.random.fold_in(_gk, 2), (200000,), 0, 12500, jnp.int32)
        dst = jnp.minimum((12500 * jax.random.uniform(jax.random.fold_in(_gk, 3), (200000,)) ** 2.0).astype(jnp.int32), 99999)
        _o = jnp.argsort(dst, stable=True)
        src = src[_o]
        dst = dst[_o]
        edge_attr_3 = 0.000844983 + 0.999762 * jax.random.normal(jax.random.fold_in(_gk, 12), (200000, 3), jnp.float32)
        edge_weight = jax.random.uniform(jax.random.fold_in(_gk, 14), (200000,), jnp.float32, 0.0, 1)
        return (x, src, dst, edge_attr_3, edge_weight)
    x, src, dst, edge_attr_3, edge_weight = _rec_inputs()

    def _L0_gnn_setup():
        import jax, jax.numpy as jnp
        import numpy as np
        N_NODES = 12500
        key = jax.random.key(seed)
        k1, k2, k3 = jax.random.split(key, 3)
        hn = jax.random.normal(k1, (N_NODES, 32), dtype=jnp.float32)
        src = jax.random.randint(k2, (200000,), 0, N_NODES, dtype=jnp.int64)
        dst = jax.random.randint(k3, (200000,), 0, N_NODES, dtype=jnp.int64)
        return {'hn': hn, 'src': src, 'dst': dst}
    _L0_gnn_all = _L0_gnn_setup()
    _L0_gnn_in = {k: v for k, v in _L0_gnn_all.items() if k in ()}
    del _L0_gnn_all

    def _L1_gnn_setup():
        import jax, jax.numpy as jnp
        import numpy as np
        from math import factorial, pi, sqrt
        MUL = 8
        RS = [(MUL, 0), (MUL, 1)]
        N_NODES = 2500
        N_EDGES = 80000
        FEAT_DIM = sum((m * (2 * l + 1) for m, l in RS))
        R_DIM = sum((mo * mi * (2 * min(lo, li) + 1) for mo, lo in RS for mi, li in RS))
        HIDDEN = 64

        def _cg(j1, j2, j3, m1, m2, m3):
            if m1 + m2 != m3:
                return 0.0
            f = factorial
            pre = sqrt((2 * j3 + 1) * f(j3 + j1 - j2) * f(j3 - j1 + j2) * f(j1 + j2 - j3) / f(j1 + j2 + j3 + 1))
            pre *= sqrt(f(j3 + m3) * f(j3 - m3) * f(j1 - m1) * f(j1 + m1) * f(j2 - m2) * f(j2 + m2))
            kmin = max(0, j2 - j3 - m1, j1 - j3 + m2)
            kmax = min(j1 + j2 - j3, j1 - m1, j2 + m2)
            s = 0.0
            for k in range(kmin, kmax + 1):
                s += (-1) ** k / (f(k) * f(j1 + j2 - j3 - k) * f(j1 - m1 - k) * f(j2 + m2 - k) * f(j3 - j2 + m1 + k) * f(j3 - j1 - m2 + k))
            return pre * s

        def _w3j_complex(l1, l2, l3):
            w = np.zeros((2 * l1 + 1, 2 * l2 + 1, 2 * l3 + 1))
            for m1 in range(-l1, l1 + 1):
                for m2 in range(-l2, l2 + 1):
                    m3 = -(m1 + m2)
                    if abs(m3) <= l3:
                        w[m1 + l1, m2 + l2, m3 + l3] = (-1) ** (l1 - l2 - m3) / sqrt(2 * l3 + 1) * _cg(l1, l2, l3, m1, m2, -m3)
            return w

        def _A(l):
            A = np.zeros((2 * l + 1, 2 * l + 1), dtype=complex)
            A[l, l] = 1.0
            for m in range(1, l + 1):
                A[l + m, l + m] = (-1) ** m / sqrt(2)
                A[l + m, l - m] = 1.0 / sqrt(2)
                A[l - m, l - m] = 1j / sqrt(2)
                A[l - m, l + m] = -1j * (-1) ** m / sqrt(2)
            return A

        def real_w3j(l1, l2, l3):
            wc = _w3j_complex(l1, l2, l3).astype(complex)
            wr = np.einsum('abc,ma,nb,oc->mno', wc, _A(l1).conj(), _A(l2).conj(), _A(l3).conj())
            i = int(np.argmax(np.abs(wr)))
            ph = wr.flat[i] / abs(wr.flat[i])
            wr = wr / ph
            assert np.abs(wr.imag).max() < 1e-10
            return np.real(wr).astype(np.float32)
        _W3J = {}
        for _mo, _lo in RS:
            for _mi, _li in RS:
                for _lf in range(abs(_lo - _li), _lo + _li + 1):
                    if (_lo, _lf, _li) not in _W3J:
                        _W3J[_lo, _lf, _li] = jnp.asarray(real_w3j(_lo, _lf, _li))
        _NORM = []
        for _mo, _lo in RS:
            _num = sum((mi * (2 * min(_lo, li) + 1) for mi, li in RS))
            _NORM.append(sqrt(4.0 * pi) * sqrt(2.0 * _lo + 1.0) / sqrt(_num))
        _F_OFFS = [0] + list(np.cumsum([mi * (2 * li + 1) for mi, li in RS]))

        def spherical_harmonics(rel_vec):
            r = rel_vec / jnp.linalg.norm(rel_vec, axis=-1, keepdims=True)
            x, y, z = (r[:, 0], r[:, 1], r[:, 2])
            y0 = jnp.full_like(x, 0.5 / sqrt(pi))[:, None]
            c1 = sqrt(3.0 / (4.0 * pi))
            y1 = c1 * jnp.stack([y, z, x], axis=-1)
            c2a = 0.5 * sqrt(15.0 / pi)
            c2b = 0.25 * sqrt(5.0 / pi)
            c2c = 0.25 * sqrt(15.0 / pi)
            y2 = jnp.stack([c2a * x * y, c2a * y * z, c2b * (3.0 * z * z - 1.0), c2a * x * z, c2c * (x * x - y * y)], axis=-1)
            return jnp.concatenate([y0, y1, y2], axis=-1)
        key = jax.random.key(seed)
        ks = jax.random.split(key, 6)
        features = jax.random.normal(ks[0], (N_NODES, FEAT_DIM), dtype=jnp.float32)
        abs_distances = jax.random.uniform(ks[1], (N_EDGES,), dtype=jnp.float32, minval=0.1, maxval=1.0)
        rel_vec = jax.random.normal(ks[2], (N_EDGES, 3), dtype=jnp.float32)
        edge_index = jax.random.randint(ks[3], (2, N_EDGES), 0, N_NODES, dtype=jnp.int32)
        w1 = jax.random.normal(ks[4], (1, HIDDEN), dtype=jnp.float32)
        b1 = jnp.zeros((HIDDEN,), jnp.float32)
        w2 = jax.random.normal(ks[5], (HIDDEN, R_DIM), dtype=jnp.float32) / sqrt(HIDDEN)
        b2 = jnp.zeros((R_DIM,), jnp.float32)
        return {'features': features, 'abs_distances': abs_distances, 'rel_vec': rel_vec, 'edge_index': edge_index, 'w1': w1, 'b1': b1, 'w2': w2, 'b2': b2}
    _L1_gnn_all = _L1_gnn_setup()
    _L1_gnn_in = {k: v for k, v in _L1_gnn_all.items() if k in ('w1', 'b1', 'w2', 'b2')}
    del _L1_gnn_all
    return {'x': x, 'src': src, 'dst': dst, 'edge_attr_3': edge_attr_3, 'edge_weight': edge_weight, 'L1_gnn_w1': _L1_gnn_in['w1'], 'L1_gnn_b1': _L1_gnn_in['b1'], 'L1_gnn_w2': _L1_gnn_in['w2'], 'L1_gnn_b2': _L1_gnn_in['b2']}

def reference(x, src, dst, edge_attr_3, edge_weight, L1_gnn_w1, L1_gnn_b1, L1_gnn_w2, L1_gnn_b2):
    import jax
    import jax.numpy as jnp

    def _L0_gnn_ref(hn, src, dst):
        import jax, jax.numpy as jnp
        import numpy as np
        N_NODES = 12500
        msgs = hn[src]
        sums = jax.ops.segment_sum(msgs, dst, num_segments=N_NODES)
        deg = jax.ops.segment_sum(jnp.ones((dst.shape[0],), dtype=hn.dtype), dst, num_segments=N_NODES)
        hn_aggr = jnp.where(deg[:, None] > 0, sums / jnp.maximum(deg[:, None], 1.0), 0.0)
        return hn_aggr

    def _L1_gnn_ref(features, abs_distances, rel_vec, edge_index, w1, b1, w2, b2):
        import jax, jax.numpy as jnp
        import numpy as np
        from math import factorial, pi, sqrt
        MUL = 8
        RS = [(MUL, 0), (MUL, 1)]
        N_NODES = 2500
        N_EDGES = 80000
        FEAT_DIM = sum((m * (2 * l + 1) for m, l in RS))
        R_DIM = sum((mo * mi * (2 * min(lo, li) + 1) for mo, lo in RS for mi, li in RS))
        HIDDEN = 64

        def _cg(j1, j2, j3, m1, m2, m3):
            if m1 + m2 != m3:
                return 0.0
            f = factorial
            pre = sqrt((2 * j3 + 1) * f(j3 + j1 - j2) * f(j3 - j1 + j2) * f(j1 + j2 - j3) / f(j1 + j2 + j3 + 1))
            pre *= sqrt(f(j3 + m3) * f(j3 - m3) * f(j1 - m1) * f(j1 + m1) * f(j2 - m2) * f(j2 + m2))
            kmin = max(0, j2 - j3 - m1, j1 - j3 + m2)
            kmax = min(j1 + j2 - j3, j1 - m1, j2 + m2)
            s = 0.0
            for k in range(kmin, kmax + 1):
                s += (-1) ** k / (f(k) * f(j1 + j2 - j3 - k) * f(j1 - m1 - k) * f(j2 + m2 - k) * f(j3 - j2 + m1 + k) * f(j3 - j1 - m2 + k))
            return pre * s

        def _w3j_complex(l1, l2, l3):
            w = np.zeros((2 * l1 + 1, 2 * l2 + 1, 2 * l3 + 1))
            for m1 in range(-l1, l1 + 1):
                for m2 in range(-l2, l2 + 1):
                    m3 = -(m1 + m2)
                    if abs(m3) <= l3:
                        w[m1 + l1, m2 + l2, m3 + l3] = (-1) ** (l1 - l2 - m3) / sqrt(2 * l3 + 1) * _cg(l1, l2, l3, m1, m2, -m3)
            return w

        def _A(l):
            A = np.zeros((2 * l + 1, 2 * l + 1), dtype=complex)
            A[l, l] = 1.0
            for m in range(1, l + 1):
                A[l + m, l + m] = (-1) ** m / sqrt(2)
                A[l + m, l - m] = 1.0 / sqrt(2)
                A[l - m, l - m] = 1j / sqrt(2)
                A[l - m, l + m] = -1j * (-1) ** m / sqrt(2)
            return A

        def real_w3j(l1, l2, l3):
            wc = _w3j_complex(l1, l2, l3).astype(complex)
            wr = np.einsum('abc,ma,nb,oc->mno', wc, _A(l1).conj(), _A(l2).conj(), _A(l3).conj())
            i = int(np.argmax(np.abs(wr)))
            ph = wr.flat[i] / abs(wr.flat[i])
            wr = wr / ph
            assert np.abs(wr.imag).max() < 1e-10
            return np.real(wr).astype(np.float32)
        _W3J = {}
        for _mo, _lo in RS:
            for _mi, _li in RS:
                for _lf in range(abs(_lo - _li), _lo + _li + 1):
                    if (_lo, _lf, _li) not in _W3J:
                        _W3J[_lo, _lf, _li] = jnp.asarray(real_w3j(_lo, _lf, _li))
        _NORM = []
        for _mo, _lo in RS:
            _num = sum((mi * (2 * min(_lo, li) + 1) for mi, li in RS))
            _NORM.append(sqrt(4.0 * pi) * sqrt(2.0 * _lo + 1.0) / sqrt(_num))
        _F_OFFS = [0] + list(np.cumsum([mi * (2 * li + 1) for mi, li in RS]))

        def spherical_harmonics(rel_vec):
            r = rel_vec / jnp.linalg.norm(rel_vec, axis=-1, keepdims=True)
            x, y, z = (r[:, 0], r[:, 1], r[:, 2])
            y0 = jnp.full_like(x, 0.5 / sqrt(pi))[:, None]
            c1 = sqrt(3.0 / (4.0 * pi))
            y1 = c1 * jnp.stack([y, z, x], axis=-1)
            c2a = 0.5 * sqrt(15.0 / pi)
            c2b = 0.25 * sqrt(5.0 / pi)
            c2c = 0.25 * sqrt(15.0 / pi)
            y2 = jnp.stack([c2a * x * y, c2a * y * z, c2b * (3.0 * z * z - 1.0), c2a * x * z, c2c * (x * x - y * y)], axis=-1)
            return jnp.concatenate([y0, y1, y2], axis=-1)
        src, dst = (edge_index[0], edge_index[1])
        R = jax.nn.relu(abs_distances[:, None] @ w1 + b1) @ w2 + b2
        Y = spherical_harmonics(rel_vec)
        Fj = features[src]
        E = Fj.shape[0]
        msg_blocks = []
        r_off = 0
        for i, (mo, lo) in enumerate(RS):
            acc = jnp.zeros((E, mo, 2 * lo + 1), dtype=features.dtype)
            for j, (mi, li) in enumerate(RS):
                n_lf = 2 * min(lo, li) + 1
                sz = mo * mi * n_lf
                Rb = R[:, r_off:r_off + sz].reshape(E, mo, mi, n_lf)
                r_off += sz
                Fb = Fj[:, _F_OFFS[j]:_F_OFFS[j + 1]].reshape(E, mi, 2 * li + 1)
                for k, lf in enumerate(range(abs(lo - li), lo + li + 1)):
                    C = _W3J[lo, lf, li]
                    Yf = Y[:, lf * lf:(lf + 1) * (lf + 1)]
                    acc = acc + _NORM[i] * jnp.einsum('euv,ef,evi,ofi->euo', Rb[..., k], Yf, Fb, C)
            msg_blocks.append(acc.reshape(E, -1))
        msg = jnp.concatenate(msg_blocks, axis=-1)
        out = jnp.zeros((features.shape[0], msg.shape[1]), dtype=features.dtype)
        out = out.at[dst].add(msg)
        return out
    edge_index = jnp.stack([src, dst])
    x = _layernorm(x + _L0_gnn_ref(x, src, dst), axis=-1)
    x = _layernorm(x + _L1_gnn_ref(x, edge_weight, edge_attr_3, edge_index, L1_gnn_w1, L1_gnn_b1, L1_gnn_w2, L1_gnn_b2), axis=-1)
    return x

_drawn_inputs = setup_inputs


def setup_inputs(seed=0):
    import zlib

    import numpy as np

    out = dict(_drawn_inputs(seed))
    spreads = {'L1_gnn_b1': (0.0, 0.1), 'L1_gnn_b2': (0.0, 0.1)}
    factors = {}
    for name, (base, spread) in spreads.items():
        noise = np.random.default_rng([zlib.crc32(name.encode()), seed]).standard_normal(out[name].shape)
        drawn = base * np.exp(spread * noise) if base else spread * noise
        out[name] = jnp.asarray(drawn.astype(out[name].dtype))
    for name, factor in factors.items():
        out[name] = (out[name] * factor).astype(out[name].dtype)
    return out
```

```python
import math
from contextlib import ExitStack

import concourse.bass as bass
from concourse import mybir

F32 = mybir.dt.float32
I32 = mybir.dt.int32
ALU = mybir.AluOpType
ACT = mybir.ActivationFunctionType
AX = mybir.AxisListType

P = 128
E = 200000
N = 12500
D = 32
MUL = 8
H = 64
RD = 6 * MUL * MUL
T = 16
COLS = 1568
BATCHES = COLS // T
PAIRS = BATCHES // 2
NPP = 98
SEG = 196
ROWS = P * COLS // SEG
RPP = COLS // SEG
SG = 4
GROUPS = T // SG
NC = 7
CHUNKS = NPP // NC
SENTINEL = 1 << 20
EPS = 1e-5
LAST = P - 1
E_REST = E - LAST * COLS
N_REST = N - LAST * NPP

C_SS = 0.25
C_SV = 0.25
C_VS = math.sqrt(3.0) / (4.0 * math.sqrt(2.0))
C_A0 = 0.25 / math.sqrt(2.0)
C_A1 = math.sqrt(3.0) / 8.0
C_A2 = 3.0 / 8.0


STEPS = {"layer0": 44, "chunks": 18, "layer1": 18}


class Steps:

    def __init__(self, eng, sem, base=0):
        self.eng, self.sem, self.base, self.n = eng, sem, base, 0

    def mark(self, ins):
        ins.then_inc(self.sem, 1)
        self.n += 1

    def settle(self):
        self.eng.wait_ge(self.sem, self.base + self.n)


def build_program(nc, x, src, dst, edge_attr, edge_weight, w1, b1, w2, b2, out):
    with ExitStack() as ctx:
        def sb(name, shape, dt=F32):
            return ctx.enter_context(nc.sbuf_tensor(name, shape, dt))

        def sem(name):
            return ctx.enter_context(nc.semaphore(name))

        def pair(name):
            return [sem(f"{name}_{k}") for k in range(2)]

        def dram(name, shape):
            return nc.dram_tensor(name, shape, F32, kind="Internal").ap()

        dst_rows = dram("dst_rows", (ROWS, SEG))
        row_last = dram("row_last", (1, ROWS))
        upto_d = dram("upto_d", (1, P * NPP + 1))
        weight_t = dram("weight_t", (COLS, P))
        frame_d = dram("frame_d", (P, COLS * 9))
        run1_d = dram("run1_d", (P * COLS, D))
        run2_d = dram("run2_d", (P * COLS, D))
        x1_d = dram("x1_d", (P * NPP, D))

        src_all = sb("src_all", [P, COLS + 2 * T], I32)
        dst_i = sb("dst_i", [P, COLS], I32)
        dst_f = sb("dst_f", [P, COLS])
        same = sb("same", [P, COLS])
        unit = sb("unit", [P, COLS, 3])
        inv_len = sb("inv_len", [P, COLS])
        w_sb = sb("w_sb", [P, COLS])
        x_sb = sb("x_sb", [P, NPP, D])
        x1_sb = sb("x1_sb", [P, NPP, D])
        ident = sb("ident", [P, P])
        node_i = sb("node_i", [P, NPP], I32)
        node = sb("node", [P, NPP])
        first_i = sb("first_i", [P, P], I32)
        first_node = sb("first_node", [P, P])
        last8 = sb("last8", [P, RPP])
        coarse = sb("coarse", [P, ROWS])
        next_first = sb("next_first", [P, 2])
        goes_on = sb("goes_on", [P, 1])
        goes_on_j = sb("goes_on_j", [P, NPP])
        upto = sb("upto", [P, NPP])
        before = sb("before", [P, NPP])
        has_edge = sb("has_edge", [P, NPP])
        inv_deg = sb("inv_deg", [P, NPP])
        pos = sb("pos", [P, NPP + 2 * NC], I32)
        w2_sb = sb("w2_sb", [H + 1, RD])
        wc = sb("wc", [H + 1, RD])
        wtmp = sb("wtmp", [H + 1, MUL * MUL])
        w1_col = sb("w1_col", [H, 1])
        b1_col = sb("b1_col", [H, 1])
        zero1 = sb("zero1", [1, 1])

        idx = [sb(f"idx{k}", [P, T], I32) for k in range(2)]
        got = [sb(f"got{k}", [P, T, D]) for k in range(2)]
        terms = [sb(f"terms{k}", [P, D, T + 1]) for k in range(2)]
        masks = [sb(f"masks{k}", [P, D, T + 1]) for k in range(2)]
        runs = [sb(f"runs{k}", [P, D, T + 1]) for k in range(2)]
        runs_t = [sb(f"runs_t{k}", [P, T, D]) for k in range(2)]
        frame = [sb(f"frame{k}", [P, T, 3, 3]) for k in range(2)]
        query = [sb(f"query{k}", [P, 1], I32) for k in range(2)]
        node_c = [sb(f"node_c{k}", [P, 1]) for k in range(2)]
        rows_below = [sb(f"rows_below{k}", [P, 1]) for k in range(2)]
        feat = [sb(f"feat{k}", [P, T, 40]) for k in range(2)]
        row = [sb(f"row{k}", [P, SEG]) for k in range(2)]
        hid = [sb(f"hid{k}", [H + 1, T * P]) for k in range(2)]
        halves = [sb(f"halves{k}", [P, SG, D, MUL]) for k in range(2)]
        pos_c = [sb(f"pos_c{k}", [P, NC], I32) for k in range(2)]
        ngot = [sb(f"ngot{k}", [P, NC, D]) for k in range(2)]
        nout = [sb(f"nout{k}", [P, NC, D]) for k in range(2)]
        pick = [sb(f"pick{k}", [P, NC, P]) for k in range(2)]
        var = [sb(f"var{k}", [P, NC]) for k in range(2)]
        sdev = [sb(f"sdev{k}", [P, NC]) for k in range(2)]
        wt_out = [sb(f"wt_out{k}", [P, P]) for k in range(2)]

        uvec = sb("uvec", [P, T, 3])
        prod = sb("prod", [P, SG, D, 2 * MUL])
        sq = prod[:, :, :, :].rearrange("p a b c -> p (a b c)")
        part = [sb(f"part{k}", [P, T, 3, MUL]) for k in range(3)]
        small = sb("small", [P, 6, T])
        junk = sb("junk", [P, ROWS])
        below = sb("below", [P, 1])
        tail = sb("tail", [P, D])
        nsq = sb("nsq", [P, NC, D])
        mean = sb("mean", [P, NC])
        rstd = sb("rstd", [P, NC])

        ps_r = ctx.enter_context(nc.psum_tensor("ps_r", [P, 2, 3, 512], F32))
        ps_m = ctx.enter_context(nc.psum_tensor("ps_m", [P, 2, 512], F32))

        pads_set = sem("pads_set")
        loaded_src = sem("loaded_src")
        loaded_dst = sem("loaded_dst")
        loaded_attr = sem("loaded_attr")
        loaded_w = sem("loaded_w")
        loaded_x = sem("loaded_x")
        loaded_net = sem("loaded_net")
        consts_made = sem("consts_made")
        pool_step = sem("pool_step")
        pool_go = sem("pool_go")
        dve_step = sem("dve_step")
        act_step = sem("act_step")
        dst_ready = sem("dst_ready")
        rows_stored = sem("rows_stored")
        coarse_loaded = sem("coarse_loaded")
        next_loaded = sem("next_loaded")
        lensq_ready = sem("lensq_ready")
        len_ready = sem("len_ready")
        same_ready = sem("same_ready")
        w_turned = sem("w_turned")
        w_copied = sem("w_copied")
        w_stored = pair("w_stored")
        wc_ready = sem("wc_ready")
        idx_ready = sem("idx_ready")
        query_ready = sem("query_ready")
        row_landed = pair("row_landed")
        row_counted = sem("row_counted")
        frame_ready = sem("frame_ready")
        frame_stored = pair("frame_stored")
        upto_ready = sem("upto_ready")
        upto_stored = sem("upto_stored")
        before_loaded = sem("before_loaded")
        got1_landed = pair("got1_landed")
        terms1_ready = sem("terms1_ready")
        masks1_ready = sem("masks1_ready")
        scanned = sem("scanned")
        runs_turned = sem("runs_turned")
        runs_stored = pair("runs_stored")
        hid_loaded = pair("hid_loaded")
        hid_ready = sem("hid_ready")
        frame_loaded = pair("frame_loaded")
        got2_landed = pair("got2_landed")
        f0_copied = sem("f0_copied")
        rotated_in = sem("rotated_in")
        negx_copied = sem("negx_copied")
        radial_ready = sem("radial_ready")
        multiplied = sem("multiplied")
        halves_ready = sem("halves_ready")
        summed = sem("summed")
        m0_copied = sem("m0_copied")
        masks2_ready = sem("masks2_ready")
        rotated_out = sem("rotated_out")
        pos_ready = [sem(f"pos_ready{k}") for k in range(2)]
        tail_ready = [sem(f"tail_ready{k}") for k in range(2)]
        ngot_landed = [pair(f"ngot_landed{k}") for k in range(2)]
        pick_ready = [sem(f"pick_ready{k}") for k in range(2)]
        carry_ready = [sem(f"carry_ready{k}") for k in range(2)]
        ngot_used = [sem(f"ngot_used{k}") for k in range(2)]
        var_ready = [sem(f"var_ready{k}") for k in range(2)]
        sdev_ready = [sem(f"sdev_ready{k}") for k in range(2)]
        nout_ready = [sem(f"nout_ready{k}") for k in range(2)]
        nout_stored = [pair(f"nout_stored{k}") for k in range(2)]

        block = ctx.enter_context(nc.Block())

        def spread(ap, axis, n):
            a = ap.unsqueeze(axis)
            shape = list(a.shape)
            shape[axis] = n
            return a.to_broadcast(shape)

        def load_nodes_or_edges(eng, tile, flat, per, done):
            full = flat[0:LAST * per].rearrange("(p t) -> p t", t=per)
            eng.dma_start(tile[0:112, 0:per], full[0:112, :]).then_inc(done, 16)
            eng.dma_start(tile[112:LAST, 0:per], full[112:LAST, :]).then_inc(done, 16)
            rest = flat.shape[0] - LAST * per
            eng.dma_start(tile[LAST:P, 0:rest], flat[LAST * per:].unsqueeze(0)).then_inc(done, 16)

        frame_rows = frame_d
        run_rows = [r.rearrange("(p t) f -> p (t f)", p=P) for r in (run1_d, run2_d)]
        x1_rows = x1_d.rearrange("(p j) f -> p (j f)", p=P)

        @block.sync
        def _(sp):
            sp.wait_ge(pads_set, 5)
            load_nodes_or_edges(sp, src_all, src, COLS, loaded_src)
            load_nodes_or_edges(sp, dst_i, dst, COLS, loaded_dst)
            load_nodes_or_edges(sp, unit[:, :, :].rearrange("p t c -> p (t c)"),
                                edge_attr.rearrange("e c -> (e c)"), 3 * COLS, loaded_attr)
            load_nodes_or_edges(sp, w_sb, edge_weight, COLS, loaded_w)
            load_nodes_or_edges(sp, x_sb[:, :, :].rearrange("p j f -> p (j f)"),
                                x.rearrange("n f -> (n f)"), NPP * D, loaded_x)
            sp.dma_start(w2_sb[0:H, :], w2).then_inc(loaded_net, 16)
            sp.dma_start(w2_sb[H:H + 1, :], b2.unsqueeze(0)).then_inc(loaded_net, 16)
            sp.dma_start(w1_col[:, :], w1.rearrange("a h -> h a")).then_inc(loaded_net, 16)
            sp.dma_start(b1_col[:, :], b1.unsqueeze(1)).then_inc(loaded_net, 16)
            sp.wait_ge(dst_ready, 2)
            sp.dma_start(dst_rows.rearrange("(p r) s -> p (r s)", p=P), dst_f[:, :]).then_inc(rows_stored, 16)
            sp.dma_start(row_last.rearrange("a (p r) -> (a p) r", p=P), last8[:, :]).then_inc(rows_stored, 16)
            sp.wait_ge(rows_stored, 32)
            sp.dma_start(coarse[:, :], row_last[0, :].partition_broadcast(P)).then_inc(coarse_loaded, 16)
            sp.dma_start(next_first[0:LAST, :], dst_rows.rearrange("(p r) s -> p (r s)", p=P)[1:P, 0:2]
                         ).then_inc(next_loaded, 16)
            for c in range((COLS + P - 1) // P):
                w = min(P, COLS - c * P)
                sp.wait_ge(w_copied, c + 1)
                sp.dma_start(weight_t[c * P:c * P + w, :], wt_out[c % 2][0:w, :]).then_inc(w_stored[c % 2], 16)

            def layer0(i):
                for k in range(2):
                    b = 2 * i + k
                    sp.wait_ge(frame_ready, b + 1)
                    sp.dma_start(frame_rows[:, bass.ds(b * (T * 9), T * 9)],
                                 frame[k][:, :, :, :].rearrange("p t c a -> p (t c a)")
                                 ).then_inc(frame_stored[k], 16)
                    sp.wait_ge(runs_turned, b + 1)
                    sp.dma_start(run_rows[0][:, bass.ds(b * (T * D), T * D)],
                                 runs_t[k][:, :, :].rearrange("p t f -> p (t f)")
                                 ).then_inc(runs_stored[k], 16)

            with sp.Fori(0, PAIRS) as i:
                layer0(i)
            sp.wait_ge(upto_ready, 1)
            sp.dma_start(upto_d[0:1, 0:1], zero1[:, :]).then_inc(upto_stored, 16)
            sp.dma_start(upto_d[0, 1:P * NPP + 1].rearrange("(p j) -> p j", p=P), upto[:, :]
                         ).then_inc(upto_stored, 16)
            sp.wait_ge(upto_stored, 32)
            sp.dma_start(before[:, :], upto_d[0, 0:P * NPP].rearrange("(p j) -> p j", p=P)
                         ).then_inc(before_loaded, 16)

            def nodes0(i):
                for k in range(2):
                    c = 2 * i + k
                    sp.wait_ge(nout_ready[0], c + 1)
                    sp.dma_start(x1_rows[:, bass.ds(c * (NC * D), NC * D)],
                                 nout[k][:, :, :].rearrange("p j f -> p (j f)")
                                 ).then_inc(nout_stored[0][k], 16)

            with sp.Fori(0, CHUNKS // 2) as i:
                nodes0(i)

            def layer1(i, first):
                for k in range(2):
                    b = 2 * i + k
                    if not first:
                        sp.wait_ge(radial_ready, GROUPS * (b - 1))
                        sp.wait_ge(rotated_out, b - 1)
                    else:
                        sp.wait_ge(w_stored[0], 16 * 7)
                        sp.wait_ge(w_stored[1], 16 * 6)
                        sp.wait_ge(frame_stored[k], 16 * PAIRS)
                    sp.dma_start(hid[k][0:H, :],
                                 weight_t[bass.ds(b * T, T), :].rearrange("t p -> (t p)").partition_broadcast(H)
                                 ).then_inc(hid_loaded[k], 16)
                    sp.dma_start(frame[k][:, :, :, :].rearrange("p t c a -> p (t c a)"),
                                 frame_rows[:, bass.ds(b * (T * 9), T * 9)]).then_inc(frame_loaded[k], 16)
                    if not first:
                        store_runs2(b - 2, k)

            def store_runs2(b, k):
                sp.wait_ge(runs_turned, BATCHES + b + 1)
                sp.dma_start(run_rows[1][:, bass.ds(b * (T * D), T * D)],
                             runs_t[k][:, :, :].rearrange("p t f -> p (t f)")).then_inc(runs_stored[k], 16)

            layer1(0, True)
            with sp.Fori(1, PAIRS) as i:
                layer1(i, False)
            store_runs2(BATCHES - 2, 0)
            store_runs2(BATCHES - 1, 1)

            out_rows = out.rearrange("n f -> (n f)")[0:LAST * NPP * D].rearrange("(p j) -> p j", p=LAST)

            def nodes1(i):
                for k in range(2):
                    c = 2 * i + k
                    sp.wait_ge(nout_ready[1], c + 1)
                    for lo, hi in ((0, 112), (112, LAST)):
                        sp.dma_start(out_rows[lo:hi, bass.ds(c * (NC * D), NC * D)],
                                     nout[k][lo:hi, :, :].rearrange("p j f -> p (j f)")
                                     ).then_inc(nout_stored[1][k], 16)

            with sp.Fori(0, CHUNKS // 2) as i:
                nodes1(i)
            sp.dma_start(out[LAST * NPP:N, :].rearrange("n f -> (n f)").unsqueeze(0),
                         x1_sb[LAST:P, 0:N_REST, :].rearrange("p j f -> p (j f)")
                         ).then_inc(nout_stored[1][0], 16)
            sp.wait_ge(nout_stored[1][0], 32 * (CHUNKS // 2) + 16)
            sp.wait_ge(nout_stored[1][1], 32 * (CHUNKS // 2))

        @block.gpsimd
        def _(pool):
            s = Steps(pool, pool_step)
            s.mark(pool.memset(ident[:, :], 0.0))
            s.settle()
            pool.affine_select(out=ident[:, :], in_=ident[:, :], compare_op=ALU.not_equal, fill=1.0,
                               base=0, pattern=[[-1, P]], channel_multiplier=1).then_inc(consts_made, 1)
            pool.iota(node_i[:, :], pattern=[[1, NPP]], base=0, channel_multiplier=NPP).then_inc(consts_made, 1)
            pool.iota(first_i[:, :], pattern=[[NPP, P]], base=0, channel_multiplier=0).then_inc(consts_made, 1)

            def layer0(i, first):
                for k in range(2):
                    b = 2 * i + k
                    pool.wait_ge(idx_ready, b + 1)
                    if not first:
                        pool.wait_ge(terms1_ready, b - 1)
                        pool.wait_ge(got1_landed[k], 16 * T * i)
                    pool.sem_inc(pool_go, 1)
                    for t in range(T):
                        pool.indirect_dma_start(got[k][:, t, :], None, x,
                                                bass.IndirectOffsetOnAxis(ap=idx[k][:, t:t + 1], axis=0)
                                                ).then_inc(got1_landed[k], 16)
                    pool.wait_ge(query_ready, b + 1)
                    if not first:
                        pool.wait_ge(row_counted, b - 1)
                    pool.sem_inc(pool_go, 1)
                    pool.indirect_dma_start(row[k][:, :], None, dst_rows,
                                            bass.IndirectOffsetOnAxis(ap=query[k][:, :], axis=0)
                                            ).then_inc(row_landed[k], 16)

            pool.wait_ge(rows_stored, 32)
            layer0(0, True)
            with pool.Fori(1, PAIRS) as i:
                layer0(i, False)

            def runs_in_dram(layer):
                pool.wait_ge(runs_stored[0], 16 * PAIRS * (layer + 1))
                pool.wait_ge(runs_stored[1], 16 * PAIRS * (layer + 1))

            def nodes_in_dram():
                pool.wait_ge(nout_stored[0][0], 16 * (CHUNKS // 2))
                pool.wait_ge(nout_stored[0][1], 16 * (CHUNKS // 2))

            def nodes(i, layer, table, first):
                for k in range(2):
                    c = 2 * i + k
                    pool.wait_ge(pos_ready[layer], c + 1)
                    if not first:
                        pool.wait_ge(ngot_used[layer], c - 1)
                    pool.sem_inc(pool_go, 1)
                    for j in range(NC):
                        pool.indirect_dma_start(ngot[k][:, j, :], None, table,
                                                bass.IndirectOffsetOnAxis(ap=pos_c[k][:, j:j + 1], axis=0)
                                                ).then_inc(ngot_landed[layer][k], 16)

            runs_in_dram(0)
            nodes(0, 0, run1_d, True)
            with pool.Fori(1, CHUNKS // 2) as i:
                nodes(i, 0, run1_d, False)

            def layer1(i, first):
                for k in range(2):
                    b = 2 * i + k
                    pool.wait_ge(idx_ready, BATCHES + b + 1)
                    if not first:
                        pool.wait_ge(rotated_in, b - 1)
                        pool.wait_ge(f0_copied, b - 1)
                    pool.sem_inc(pool_go, 1)
                    for t in range(T):
                        pool.indirect_dma_start(got[k][:, t, :], None, x1_d,
                                                bass.IndirectOffsetOnAxis(ap=idx[k][:, t:t + 1], axis=0)
                                                ).then_inc(got2_landed[k], 16)

            nodes_in_dram()
            layer1(0, True)
            with pool.Fori(1, PAIRS) as i:
                layer1(i, False)
            runs_in_dram(1)
            nodes(0, 1, run2_d, True)
            with pool.Fori(1, CHUNKS // 2) as i:
                nodes(i, 1, run2_d, False)

        @block.scalar
        def _(act):
            act.wait_ge(lensq_ready, 1)
            act.activation(inv_len[:, :], inv_len[:, :], ACT.Sqrt).then_inc(len_ready, 1)
            for c in range((COLS + P - 1) // P):
                w = min(P, COLS - c * P)
                act.wait_ge(w_turned, c + 1)
                if c >= 2:
                    act.wait_ge(w_stored[c % 2], 16 * (c // 2))
                act.copy(wt_out[c % 2][0:w, :], ps_m[0:w, c % 2, 0:P]).then_inc(w_copied, 1)

            def spread_masks(b, k, done):
                act.copy(masks[k][:, :, 1:T + 1],
                         spread(same[:, bass.ds(b * T, T)], 1, D)).then_inc(done, 1)

            def turn_runs(k, done):
                act.copy(runs_t[k][:, :, :], runs[k][:, :, 1:T + 1].rearrange("p f t -> p t f")
                         ).then_inc(done, 1)

            def layer0(i, first):
                for k in range(2):
                    b = 2 * i + k
                    act.wait_ge(same_ready, 1)
                    if not first:
                        act.wait_ge(scanned, b - 1)
                    spread_masks(b, k, masks1_ready)
                    act.wait_ge(got1_landed[k], 16 * T * (i + 1))
                    act.copy(terms[k][:, :, 1:T + 1], got[k][:, :, :].rearrange("p t f -> p f t")
                             ).then_inc(terms1_ready, 1)
                    act.wait_ge(scanned, b + 1)
                    if not first:
                        act.wait_ge(runs_stored[k], 16 * i)
                    turn_runs(k, runs_turned)

            layer0(0, True)
            with act.Fori(1, PAIRS) as i:
                layer0(i, False)

            def nodes(layer):
                with act.Fori(0, CHUNKS // 2) as i:
                    for k in range(2):
                        c = 2 * i + k
                        act.wait_ge(var_ready[layer], c + 1)
                        act.activation(sdev[k][:, :], var[k][:, :], ACT.Sqrt).then_inc(sdev_ready[layer], 1)

            nodes(0)

            def finish(b, k, stores):
                act.wait_ge(summed, GROUPS * (b + 1))
                act.wait_ge(scanned, BATCHES + b - 1)
                act.copy(terms[k][:, 0:MUL, 1:T + 1],
                         ps_m[:, k, :].rearrange("p (t o) -> p o t", o=D)[:, 0:MUL, :]).then_inc(m0_copied, 1)
                spread_masks(b, k, masks2_ready)
                act.wait_ge(scanned, BATCHES + b + 1)
                act.wait_ge(runs_stored[k], 16 * (PAIRS + stores))
                turn_runs(k, runs_turned)

            def layer1(i, first):
                for k in range(2):
                    b = 2 * i + k
                    act.wait_ge(hid_loaded[k], 16 * (i + 1))
                    act.activation(hid[k][0:H, :], hid[k][0:H, :], ACT.Relu, bias=b1_col[:, :],
                                   scale=w1_col[:, :]).then_inc(hid_ready, 1)
                    act.wait_ge(got2_landed[k], 16 * T * (i + 1))
                    if not first:
                        act.wait_ge(multiplied, GROUPS * (b - 1))
                    act.copy(feat[k][:, :, 0:MUL], got[k][:, :, 0:MUL]).then_inc(f0_copied, 1)
                    act.wait_ge(rotated_in, b + 1)
                    act.activation(feat[k][:, :, 4 * MUL:5 * MUL], feat[k][:, :, 2 * MUL:3 * MUL], ACT.Copy,
                                   scale=-1.0).then_inc(negx_copied, 1)
                    if k == 1:
                        finish(b - 1, 0, i)
                    elif not first:
                        finish(b - 1, 1, i - 1)

            act.wait_ge(loaded_net, 64)
            layer1(0, True)
            with act.Fori(1, PAIRS) as i:
                layer1(i, False)
            finish(BATCHES - 1, 1, PAIRS - 1)
            nodes(1)

        @block.tensor
        def _(pe):
            pe.wait_ge(loaded_w, 48)
            pe.wait_ge(consts_made, 3)
            turns = (COLS + P - 1) // P
            for c in range(turns):
                w = min(P, COLS - c * P)
                if c >= 2:
                    pe.wait_ge(w_copied, c - 1)
                pe.transpose(ps_m[0:w, c % 2, 0:P], w_sb[:, c * P:c * P + w], ident[:, :]).then_inc(w_turned, 1)
            pe.wait_ge(w_copied, turns)

            def nodes(i, layer, first):
                for k in range(2):
                    c = 2 * i + k
                    pe.wait_ge(pick_ready[layer], c + 1)
                    if not first:
                        pe.wait_ge(ngot_used[layer], c - 1)
                    for j in range(NC):
                        mm = pe.matmul(ps_m[:, k, j * D:(j + 1) * D], pick[k][:, j, :], tail[:, :],
                                       start=True, stop=True)
                    mm.then_inc(carry_ready[layer], 1)

            pe.wait_ge(tail_ready[0], 1)
            nodes(0, 0, True)
            with pe.Fori(1, CHUNKS // 2) as i:
                nodes(i, 0, False)

            def add_halves(b, k, g, free):
                pe.wait_ge(halves_ready, GROUPS * b + g + 1)
                if free is not None:
                    pe.wait_ge(free[0], free[1])
                    pe.wait_ge(free[2], free[3])
                for v in range(MUL):
                    mm = pe.matmul(ps_m[:, k, g * SG * D:(g + 1) * SG * D], ident[:, :],
                                   halves[g % 2][:, :, :, v].rearrange("p t o -> p (t o)"),
                                   start=(v == 0), stop=(v == MUL - 1))
                mm.then_inc(summed, 1)

            def layer1(i, first):
                for k in range(2):
                    b = 2 * i + k
                    pe.wait_ge(hid_ready, b + 1)
                    for g in range(GROUPS):
                        if not (first and k == 0 and g < 2):
                            pe.wait_ge(multiplied, GROUPS * b + g - 1)
                        for t in range(SG):
                            col = (g * SG + t) * P
                            h = hid[k][:, col:col + P]
                            pe.matmul(ps_r[:, g % 2, t // 2, 256 * (t % 2):256 * (t % 2) + 256], h,
                                      wc[:, 0:256], start=True, stop=True)
                            mm = pe.matmul(ps_r[:, g % 2, 2, 128 * t:128 * t + 128], h, wc[:, 256:384],
                                           start=True, stop=True)
                        mm.then_inc(radial_ready, 1)
                        if g:
                            add_halves(b, k, g - 1, (rotated_out, b - 1, m0_copied, b - 1)
                                       if g == 1 and not first else None)
                        elif not (first and k == 0):
                            add_halves(b - 1, 1 - k, GROUPS - 1, None)

            pe.wait_ge(wc_ready, 1)
            pe.wait_ge(ngot_used[0], CHUNKS)
            layer1(0, True)
            with pe.Fori(1, PAIRS) as i:
                layer1(i, False)
            add_halves(BATCHES - 1, 1, GROUPS - 1, None)

            pe.wait_ge(tail_ready[1], 1)
            nodes(0, 1, True)
            with pe.Fori(1, CHUNKS // 2) as i:
                nodes(i, 1, False)

        @block.vector
        def _(dve):
            s = Steps(dve, dve_step)

            def copy_idx(b, k):
                dve.tensor_scalar(idx[k][:, :], src_all[:, bass.ds(b * T, T)], 0.0, None, ALU.add).then_inc(idx_ready, 1)

            dve.memset(src_all[96:P, E_REST:COLS], 0).then_inc(pads_set, 1)
            dve.memset(dst_i[96:P, E_REST:COLS], SENTINEL).then_inc(pads_set, 1)
            dve.memset(unit[96:P, E_REST:COLS, :], 1.0).then_inc(pads_set, 1)
            dve.memset(w_sb[96:P, E_REST:COLS], 0.0).then_inc(pads_set, 1)
            dve.memset(x_sb[96:P, N_REST:NPP, :], 0.0).then_inc(pads_set, 1)
            s.mark(dve.memset(zero1[:, :], 0.0))
            s.mark(dve.memset(next_first[:, :], -1.0))
            s.mark(dve.memset(same[:, 0:1], 0.0))
            s.mark(dve.memset(runs[1][:, :, T:T + 1], 0.0))
            for k in range(2):
                s.mark(dve.memset(masks[k][:, :, 0:1], 0.0))
                s.mark(dve.memset(hid[k][H:H + 1, :], 1.0))
            s.settle()
            dve.wait_ge(loaded_src, 48)
            for k in range(2):
                copy_idx(k, k)
            s.mark(dve.tensor_copy(src_all[:, COLS:COLS + 2 * T], src_all[:, 0:2 * T]))
            dve.wait_ge(loaded_dst, 48)
            dve.tensor_copy(dst_f[:, :], dst_i[:, :]).then_inc(dst_ready, 1)
            dve.wait_ge(dst_ready, 1)
            dve.tensor_copy(last8[:, :], dst_f[:, SEG - 1::SEG]).then_inc(dst_ready, 1)
            dve.tensor_tensor(same[:, 1:COLS], dst_f[:, 1:COLS], dst_f[:, 0:COLS - 1], ALU.is_equal
                              ).then_inc(same_ready, 1)
            dve.wait_ge(consts_made, 3)
            s.mark(dve.tensor_copy(node[:, :], node_i[:, :]))
            s.mark(dve.tensor_copy(first_node[:, :], first_i[:, :]))
            dve.wait_ge(loaded_attr, 48)
            step = COLS // 4
            for c in range(4):
                u = unit[:, c * step:(c + 1) * step, :]
                v = sq[:, 0:3 * step].rearrange("p (t c) -> p t c", c=3)
                s.settle()
                s.mark(dve.tensor_tensor(v, u, u, ALU.mult))
                s.settle()
                ins = dve.tensor_reduce(inv_len[:, c * step:(c + 1) * step], v, AX.X, ALU.add)
                if c < 3:
                    s.mark(ins)
            ins.then_inc(lensq_ready, 1)
            dve.wait_ge(loaded_net, 64)
            blocks = w2_sb[:, 0:3 * MUL * MUL].rearrange("h (q u v) -> h q u v", q=3, u=MUL)
            vec = w2_sb[:, 3 * MUL * MUL:RD].rearrange("h (u v m) -> h u v m", u=MUL, m=3)
            along = wc[:, 0:256].rearrange("h (u v) -> h u v", u=2 * MUL)
            across = wc[:, 256:384].rearrange("h (u v) -> h u v", u=MUL)
            a0 = wtmp[:, :].rearrange("h (u v) -> h u v", u=MUL)
            s.mark(dve.tensor_scalar(a0, vec[:, :, :, 0], C_A0, None, ALU.mult))
            s.mark(dve.tensor_scalar(along[:, 0:MUL, 0:MUL], blocks[:, 0], C_SS, None, ALU.mult))
            s.mark(dve.tensor_scalar(along[:, 0:MUL, MUL:2 * MUL], blocks[:, 1], C_SV, None, ALU.mult))
            s.mark(dve.tensor_scalar(along[:, MUL:2 * MUL, 0:MUL], blocks[:, 2], C_VS, None, ALU.mult))
            s.mark(dve.tensor_scalar(across[:, :, MUL:2 * MUL], vec[:, :, :, 1], -C_A1, None, ALU.mult))
            s.settle()
            s.mark(dve.scalar_tensor_tensor(along[:, MUL:2 * MUL, MUL:2 * MUL], vec[:, :, :, 2],
                                            C_A2 * 2.0 / 3.0, a0, ALU.mult, ALU.add))
            dve.scalar_tensor_tensor(across[:, :, 0:MUL], vec[:, :, :, 2], -C_A2 / 3.0, a0,
                                     ALU.mult, ALU.add).then_inc(wc_ready, 1)
            dve.wait_ge(len_ready, 1)
            s.mark(dve.reciprocal(inv_len[:, :], inv_len[:, :]))
            s.settle()
            s.mark(dve.tensor_tensor(unit[:, :, :], unit[:, :, :], spread(inv_len[:, :], 2, 3), ALU.mult))
            s.settle()

            def find_row(b, k):
                s.mark(dve.tensor_scalar(node_c[k][:, :], node[:, bass.ds(b, 1)], 0.0, None, ALU.add))
                s.settle()
                s.mark(dve.tensor_scalar(junk[:, :], coarse[:, :], node_c[k][:, 0:1], None, ALU.is_le,
                                         ALU.add, accum_out=rows_below[k][:, :]))
                s.settle()
                dve.tensor_copy(query[k][:, :], rows_below[k][:, :]).then_inc(query_ready, 1)

            def count_row(b, k, landed):
                dve.wait_ge(row_landed[k], 16 * landed)
                dve.tensor_scalar(junk[:, 0:SEG], row[k][:, :], node_c[k][:, 0:1], None, ALU.is_le,
                                  ALU.add, accum_out=below[:, :]).then_inc(row_counted, 1)
                dve.wait_ge(row_counted, b + 1)
                s.mark(dve.scalar_tensor_tensor(upto[:, bass.ds(b, 1)], rows_below[k][:, :], float(SEG),
                                                below[:, :], ALU.mult, ALU.add))

            def make_frame(b, k):
                cut = unit[:, bass.ds(b * T, T), :]
                s.mark(dve.tensor_scalar(uvec[:, :, :], cut, 0.0, None, ALU.add))
                s.settle()
                n0, n1, n2 = (uvec[:, :, c] for c in (1, 2, 0))
                f = frame[k]
                sign, inv, n0i, n1i, sn0, q = (small[:, c, :] for c in range(6))
                s.mark(dve.tensor_scalar(sign, n2, 0.0, 2.0, ALU.is_ge, ALU.mult))
                s.settle()
                s.mark(dve.tensor_scalar(sign, sign, -1.0, None, ALU.add))
                s.settle()
                s.mark(dve.tensor_tensor(inv, sign, n2, ALU.add))
                s.mark(dve.tensor_tensor(sn0, sign, n0, ALU.mult))
                s.settle()
                s.mark(dve.reciprocal(inv, inv))
                s.settle()
                s.mark(dve.tensor_tensor(n0i, n0, inv, ALU.mult))
                s.mark(dve.tensor_tensor(n1i, n1, inv, ALU.mult))
                s.settle()
                s.mark(dve.tensor_tensor(q, sn0, n0i, ALU.mult))
                s.mark(dve.tensor_tensor(f[:, :, 0, 2], n1, n0i, ALU.mult))
                s.mark(dve.tensor_tensor(f[:, :, 1, 2], n1, n1i, ALU.mult))
                s.settle()
                s.mark(dve.scalar_tensor_tensor(f[:, :, 1, 1], f[:, :, 0, 2], -1.0, sign, ALU.mult, ALU.mult))
                s.mark(dve.tensor_scalar(f[:, :, 0, 1], q, -1.0, 1.0, ALU.mult, ALU.add))
                s.mark(dve.tensor_tensor(f[:, :, 1, 2], sign, f[:, :, 1, 2], ALU.subtract))
                s.settle()
                s.mark(dve.tensor_scalar(f[:, :, 0, 2], f[:, :, 0, 2], -1.0, None, ALU.mult))
                s.mark(dve.tensor_scalar(f[:, :, 2, 1], sn0, -1.0, None, ALU.mult))
                s.mark(dve.tensor_scalar(f[:, :, 2, 2], n1, -1.0, None, ALU.mult))
                s.mark(dve.tensor_copy(f[:, :, 0:2, 0], uvec[:, :, 1:3]))
                dve.tensor_copy(f[:, :, 2, 0], n2).then_inc(frame_ready, 1)

            def scan(b, k):
                s.mark(dve.tensor_copy(terms[k][:, :, 0:1], runs[1 - k][:, :, T:T + 1]))
                s.settle()
                dve.tensor_tensor_scan(runs[k][:, :, :].rearrange("p f t -> p (f t)"),
                                       masks[k][:, :, :].rearrange("p f t -> p (f t)"),
                                       terms[k][:, :, :].rearrange("p f t -> p (f t)"),
                                       0.0, ALU.mult, ALU.add).then_inc(scanned, 1)

            def layer0(i, first):
                for k in range(2):
                    b = 2 * i + k
                    if not first:
                        dve.wait_ge(row_landed[k], 16 * i)
                    find_row(b, k)
                    if k == 1:
                        count_row(b - 1, 0, i + 1)
                    elif not first:
                        count_row(b - 1, 1, i)
                    if not first:
                        dve.wait_ge(frame_stored[k], 16 * i)
                    make_frame(b, k)
                    if not (first and k == 0):
                        dve.wait_ge(scanned, b)
                    dve.wait_ge(terms1_ready, b + 1)
                    dve.wait_ge(masks1_ready, b + 1)
                    if not first:
                        dve.wait_ge(runs_turned, b - 1)
                    scan(b, k)
                    dve.wait_ge(got1_landed[k], 16 * T * (i + 1))
                    copy_idx(b + 2, k)

            def loop(body, count):
                s.base, s.n = s.base + s.n, 0
                body(0, True)
                start = s.base + s.n
                per = STEPS[body.__name__]
                with dve.Fori(1, count) as i:
                    s.base, s.n = start + (i - 1) * per, 0
                    body(i, False)
                    assert s.n == per, (body.__name__, s.n)
                s.base, s.n = start + (count - 1) * per, 0

            dve.wait_ge(coarse_loaded, 16)
            loop(layer0, PAIRS)
            count_row(BATCHES - 1, 1, PAIRS)
            s.settle()
            dve.tensor_copy(upto[:, 0:1], upto[:, 0:1]).then_inc(upto_ready, 1)

            dve.wait_ge(next_loaded, 16)
            s.mark(dve.tensor_tensor(goes_on[:, :], dst_f[:, COLS - 1:COLS], next_first[:, 0:1], ALU.is_equal))
            s.mark(dve.tensor_scalar(below[:, :], dst_f[:, COLS - 1:COLS], 1.0, None, ALU.add))
            s.settle()
            s.mark(dve.tensor_tensor(goes_on[:, :], goes_on[:, :], below[:, :], ALU.mult))
            s.settle()
            s.mark(dve.tensor_scalar(goes_on[:, :], goes_on[:, :], -1.0, None, ALU.add))
            s.mark(dve.tensor_scalar(goes_on_j[:, :], node[:, :], node[:, 0:1], None, ALU.subtract))
            s.settle()
            s.mark(dve.tensor_scalar(goes_on_j[:, :], goes_on_j[:, :], goes_on[:, 0:1], -1.0, ALU.subtract, ALU.mult))
            s.mark(dve.tensor_scalar(inv_deg[:, :], upto[:, :], -1.0, 0.0, ALU.add, ALU.max))
            s.settle()
            s.mark(dve.memset(pos[:, NPP:NPP + 2 * NC], 0))
            s.mark(dve.tensor_copy(pos[:, 0:NPP], inv_deg[:, :]))
            dve.wait_ge(before_loaded, 16)
            s.mark(dve.tensor_tensor(before[:, :], upto[:, :], before[:, :], ALU.subtract))
            s.settle()
            s.mark(dve.tensor_scalar(has_edge[:, :], before[:, :], 1.0, None, ALU.min))
            s.mark(dve.tensor_scalar(before[:, :], before[:, :], 1.0, None, ALU.max))
            s.settle()
            s.mark(dve.reciprocal(inv_deg[:, :], before[:, :]))
            s.settle()
            s.mark(dve.tensor_tensor(inv_deg[:, :], inv_deg[:, :], has_edge[:, :], ALU.mult))
            s.settle()

            def nodes(layer):
                weight = (inv_deg, has_edge)[layer]
                old = (x_sb, x1_sb)[layer]
                
                def copy_pos(c, k):
                    dve.tensor_scalar(pos_c[k][:, :], pos[:, bass.ds(c * NC, NC)], 0.0, None, ALU.add).then_inc(pos_ready[layer], 1)

                def chunks(i, first):
                    for k in range(2):
                        c = 2 * i + k
                        cut = bass.ds(c * NC, NC)
                        dve.tensor_tensor(pick[k][:, :, :], spread(first_node[:, :], 1, NC),
                                          spread(goes_on_j[:, cut], 2, P), ALU.is_equal
                                          ).then_inc(pick_ready[layer], 1)
                        dve.wait_ge(ngot_landed[layer][k], 16 * NC * (i + 1))
                        copy_pos(c + 2, k)
                        dve.wait_ge(carry_ready[layer], c + 1)
                        if not first:
                            dve.wait_ge(nout_stored[layer][k], (16, 32)[layer] * i)
                        o = nout[k][:, :, :]
                        dve.tensor_tensor(o, ngot[k][:, :, :],
                                          ps_m[:, k, 0:NC * D].rearrange("p (j f) -> p j f", f=D), ALU.add
                                          ).then_inc(ngot_used[layer], 1)
                        dve.wait_ge(ngot_used[layer], c + 1)
                        s.mark(dve.tensor_tensor(o, o, spread(weight[:, cut], 2, D), ALU.mult))
                        s.settle()
                        s.mark(dve.tensor_tensor(o, o, old[:, cut, :], ALU.add))
                        s.settle()
                        s.mark(dve.tensor_reduce(mean[:, :], o, AX.X, ALU.add))
                        s.settle()
                        s.mark(dve.tensor_scalar(mean[:, :], mean[:, :], -1.0 / D, None, ALU.mult))
                        s.settle()
                        s.mark(dve.tensor_tensor(o, o, spread(mean[:, :], 2, D), ALU.add))
                        s.settle()
                        s.mark(dve.tensor_tensor(nsq[:, :, :], o, o, ALU.mult))
                        s.settle()
                        s.mark(dve.tensor_reduce(var[k][:, :], nsq[:, :, :], AX.X, ALU.add))
                        s.settle()
                        dve.tensor_scalar(var[k][:, :], var[k][:, :], 1.0 / D, EPS, ALU.mult, ALU.add
                                          ).then_inc(var_ready[layer], 1)
                        dve.wait_ge(sdev_ready[layer], c + 1)
                        s.mark(dve.reciprocal(rstd[:, :], sdev[k][:, :]))
                        s.settle()
                        s.mark(dve.tensor_tensor(o, o, spread(rstd[:, :], 2, D), ALU.mult))
                        s.settle()
                        dve.tensor_scalar(x1_sb[:, cut, :], o, 0.0, None, ALU.add).then_inc(nout_ready[layer], 1)

                dve.wait_ge(scanned, BATCHES * (layer + 1))
                dve.tensor_copy(tail[:, :], runs[1][:, :, T]).then_inc(tail_ready[layer], 1)
                for k in range(2):
                    copy_pos(k, k)
                loop(chunks, CHUNKS // 2)

            dve.wait_ge(loaded_x, 48)
            nodes(0)
            dve.wait_ge(tail_ready[0], 1)
            s.mark(dve.memset(runs[1][:, :, T:T + 1], 0.0))
            s.settle()

            def finish(b, k):
                dve.wait_ge(m0_copied, b + 1)
                dve.wait_ge(summed, GROUPS * (b + 1))
                m = ps_m[:, k, :].rearrange("p (t o) -> p t o", o=D)
                for a in range(3):
                    s.mark(dve.tensor_tensor(part[a][:, :, :, :], spread(m[:, :, MUL * (a + 1):MUL * (a + 2)], 2, 3),
                                             spread(frame[k][:, :, :, a], 3, MUL), ALU.mult))
                s.settle()
                s.mark(dve.tensor_tensor(part[0][:, :, :, :], part[0][:, :, :, :], part[1][:, :, :, :], ALU.add))
                s.settle()
                dve.tensor_tensor(terms[k][:, MUL:D, 1:T + 1].rearrange("p (u i) t -> p t i u", i=3),
                                  part[0][:, :, :, :], part[2][:, :, :, :], ALU.add).then_inc(rotated_out, 1)
                dve.wait_ge(rotated_out, b + 1)
                dve.wait_ge(masks2_ready, b + 1)
                dve.wait_ge(scanned, BATCHES + b)
                dve.wait_ge(runs_turned, BATCHES + b - 1)
                scan(b, k)

            def layer1(i, first):
                for k in range(2):
                    b = 2 * i + k
                    dve.wait_ge(got2_landed[k], 16 * T * (i + 1))
                    dve.wait_ge(frame_loaded[k], 16 * (i + 1))
                    f1 = got[k][:, :, MUL:D].rearrange("p t (v c) -> p t v c", c=3)
                    for c in range(3):
                        s.mark(dve.tensor_tensor(part[c][:, :, :, :], spread(f1[:, :, :, c], 2, 3),
                                                 spread(frame[k][:, :, c, :], 3, MUL), ALU.mult))
                    s.settle()
                    s.mark(dve.tensor_tensor(part[0][:, :, :, :], part[0][:, :, :, :], part[1][:, :, :, :], ALU.add))
                    s.settle()
                    dve.tensor_tensor(feat[k][:, :, MUL:4 * MUL].rearrange("p t (a v) -> p t a v", a=3),
                                      part[0][:, :, :, :], part[2][:, :, :, :], ALU.add).then_inc(rotated_in, 1)
                    copy_idx(b + 2, k)
                    dve.wait_ge(f0_copied, b + 1)
                    dve.wait_ge(rotated_in, b + 1)
                    for g in range(GROUPS):
                        f = feat[k][:, SG * g:SG * (g + 1), :]
                        q = g % 2
                        dve.wait_ge(radial_ready, GROUPS * b + g + 1)
                        if not (first and k == 0 and g == 0):
                            dve.wait_ge(halves_ready, GROUPS * b + g)
                        dve.tensor_tensor(prod[:, :, 0:2 * MUL, :],
                                          ps_r[:, q, 0:2, :].rearrange("p n (t u v) -> p (n t) u v", t=2, u=2 * MUL),
                                          spread(f[:, :, 0:2 * MUL], 2, 2 * MUL), ALU.mult)
                        across = ps_r[:, q, 2, :].rearrange("p (t u v) -> p t u v", t=SG, u=MUL)
                        dve.tensor_tensor(prod[:, :, 2 * MUL:3 * MUL, :], across,
                                          spread(f[:, :, 2 * MUL:4 * MUL], 2, MUL), ALU.mult)
                        if g == 0:
                            dve.wait_ge(negx_copied, b + 1)
                        dve.tensor_tensor(prod[:, :, 3 * MUL:4 * MUL, :], across,
                                          spread(f[:, :, 3 * MUL:5 * MUL], 2, MUL), ALU.mult
                                          ).then_inc(multiplied, 1)
                        dve.wait_ge(multiplied, GROUPS * b + g + 1)
                        if not (first and k == 0 and g < 2):
                            dve.wait_ge(summed, GROUPS * b + g - 1)
                        dve.tensor_tensor(halves[q][:, :, :, :], prod[:, :, :, 0:MUL], prod[:, :, :, MUL:2 * MUL],
                                          ALU.add).then_inc(halves_ready, 1)
                        if g == 0 and not (first and k == 0):
                            finish(b - 1, 1 - k)

            loop(layer1, PAIRS)
            finish(BATCHES - 1, 1)
            nodes(1)


_INS = ['x', 'src', 'dst', 'edge_attr_3', 'edge_weight', 'L1_gnn_w1', 'L1_gnn_b1', 'L1_gnn_w2', 'L1_gnn_b2']


def kernel(**inputs):
    import numpy as _np
    import concourse.bacc as _bacc
    from concourse import mybir as _mybir
    from concourse.bass_utils import run_bass_kernel_spmd as _run

    nc = _bacc.Bacc("TRN2", target_bir_lowering=False, num_devices=1)
    arrays, args = {}, []
    for name in _INS:
        a = _np.ascontiguousarray(inputs[name])
        arrays[f"in_{name}_dram"] = a
        args.append(nc.dram_tensor(f"in_{name}_dram", a.shape, _mybir.dt.from_np(a.dtype), kind="ExternalInput").ap())
    args.append(nc.dram_tensor("out_0_dram", (N, D), _mybir.dt.float32, kind="ExternalOutput").ap())
    build_program(nc, *args)
    r = _run(nc, [arrays], core_ids=[0])
    return r.results[0]["out_0_dram"]
```
